# Optimizing a Trainium2 kernel written in Bass

```python
import numpy as np
import jax
import jax.numpy as jnp

def _softmax(x, axis=-1):
    return jax.nn.softmax(x, axis=axis)

def _gelu(x):
    return jax.nn.gelu(x, approximate=True)

def _silu(x):
    return jax.nn.silu(x)

def _sigmoid(x):
    return jax.nn.sigmoid(x)

def _layernorm(x, axis=-1, eps=1e-05):
    m = jnp.mean(x, axis=axis, keepdims=True)
    v = jnp.var(x, axis=axis, keepdims=True)
    return (x - m) / jnp.sqrt(v + eps)

def _scatter_add(tgt, idx, src, axis=0):
    return tgt.at[idx].add(src)

def _segment_sum(src, seg, n):
    return jax.ops.segment_sum(src, seg, n)
kernel_name = 'mk_cond_resid_d2_seqx_r2_8ccaf8'

def setup_inputs(seed: int=0):
    np.random.seed(seed)
    _w = jnp.asarray

    def _rec_inputs():
        import jax
        import jax.numpy as jnp
        _rk = jax.random.key(seed)
        x = -0.000125 + 0.9999 * jax.random.normal(jax.random.fold_in(_rk, 1), (8, 512, 2048), jnp.float32)
        _lenS = 512 - jax.random.randint(jax.random.fold_in(_rk, 7), (8,), 0, max(1, 512 // 4) + 1, jnp.int32)
        _lenS2 = 512 - jax.random.randint(jax.random.fold_in(_rk, 8), (8,), 0, max(1, 512 // 4) + 1, jnp.int32)
        itok_B_3_7 = jax.random.randint(jax.random.fold_in(_rk, 11), (8,), 3, 8, jnp.int32)
        return (x, itok_B_3_7)
    x, itok_B_3_7 = _rec_inputs()

    def _L0_cond_setup():
        import jax, jax.numpy as jnp
        import numpy as np
        MAX_LORAS, OUT, IN = (8, 2048, 2048)
        B, S = (4, 1024)
        key = jax.random.key(seed)
        k1, k2, k3 = jax.random.split(key, 3)
        x = jax.random.normal(k1, (B, S, IN), dtype=jnp.float32)
        weight = jax.random.normal(k2, (MAX_LORAS, OUT, IN), dtype=jnp.float32) * 0.02
        adapter_ids = jax.random.randint(k3, (B,), 0, MAX_LORAS, dtype=jnp.int32)
        return {'x': x, 'weight': weight, 'adapter_ids': adapter_ids}
    _L0_cond_all = _L0_cond_setup()
    _L0_cond_in = {k: v for k, v in _L0_cond_all.items() if k in ('weight',)}
    del _L0_cond_all

    def _L1_cond_setup():
        import jax, jax.numpy as jnp
        import numpy as np
        RANK = 16
        ALPHA = 16.0
        SCALING = ALPHA / RANK
        N_ADAPTERS = 8
        IN_F = 2048
        OUT_F = 2048
        BATCH = 4
        SEQ = 1024
        key = jax.random.key(seed)
        kx, ka, kb, ki = jax.random.split(key, 4)
        x = jax.random.normal(kx, (BATCH, SEQ, IN_F), dtype=jnp.float32)
        A = jax.random.normal(ka, (N_ADAPTERS, OUT_F, RANK), dtype=jnp.float32) * 0.02
        B = jax.random.normal(kb, (N_ADAPTERS, RANK, IN_F), dtype=jnp.float32) * 0.02
        adapter_ids = jax.random.randint(ki, (BATCH,), 0, N_ADAPTERS, dtype=jnp.int32)
        return {'x': x, 'A': A, 'B': B, 'adapter_ids': adapter_ids}
    _L1_cond_all = _L1_cond_setup()
    _L1_cond_in = {k: v for k, v in _L1_cond_all.items() if k in ('A', 'B')}
    del _L1_cond_all
    return {'x': x, 'itok_B_3_7': itok_B_3_7, 'L0_cond_weight': _L0_cond_in['weight'], 'L1_cond_A': _L1_cond_in['A'], 'L1_cond_B': _L1_cond_in['B']}

def reference(x, itok_B_3_7, L0_cond_weight, L1_cond_A, L1_cond_B):
    import jax
    import jax.numpy as jnp

    def _L0_cond_ref(x, weight, adapter_ids):
        import jax, jax.numpy as jnp
        import numpy as np
        MAX_LORAS, OUT, IN = (8, 2048, 2048)
        B, S = (4, 1024)
        w = weight[adapter_ids]
        return jnp.einsum('bsi,boi->bso', x, w)

    def _L1_cond_ref(x, A, B, adapter_ids):
        import jax, jax.numpy as jnp
        import numpy as np
        RANK = 16
        ALPHA = 16.0
        SCALING = ALPHA / RANK
        N_ADAPTERS = 8
        IN_F = 2048
        OUT_F = 2048
        BATCH = 4
        SEQ = 1024
        B_sel = B[adapter_ids]
        A_sel = A[adapter_ids]
        Bx = jnp.einsum('bni,bri->bnr', x, B_sel)
        out = jnp.einsum('bnr,bor->bno', Bx, A_sel)
        return out * SCALING
    x = x + _L0_cond_ref(x, L0_cond_weight, itok_B_3_7)
    x = x + _L1_cond_ref(x, L1_cond_A, L1_cond_B, itok_B_3_7)
    return x

_drawn_inputs = setup_inputs


def setup_inputs(seed=0):
    import zlib

    import numpy as np

    out = dict(_drawn_inputs(seed))
    spreads = {}
    factors = {}
    for name, (base, spread) in spreads.items():
        noise = np.random.default_rng([zlib.crc32(name.encode()), seed]).standard_normal(out[name].shape)
        drawn = base * np.exp(spread * noise) if base else spread * noise
        out[name] = jnp.asarray(drawn.astype(out[name].dtype))
    for name, factor in factors.items():
        out[name] = (out[name] * factor).astype(out[name].dtype)
    return out
```

```python
import numpy as np
import concourse.bass as bass
from concourse import mybir
from contextlib import ExitStack

P = 128
BATCH, TOKENS, FEAT = 8, 512, 2048
ADAPTERS, RANK = 8, 16
TILES = FEAT // P
CHUNKS = FEAT // P
PAIRS = TILES // 2
BLOCKS = 4
KB = CHUNKS // BLOCKS
BLOCK_COLS = KB * 2 * P
GROUP_COLS = KB * TOKENS
REP = P // (2 * RANK)
HALF = P // 2
BX_AT, A_AT = 6, 10


def low_rank_chain(nc, ids, xT, wT, bT, aT, outT):
    f32, f32r = mybir.dt.float32, mybir.dt.float32r
    COPY = mybir.ActivationFunctionType.Copy
    ADD, SUB = mybir.AluOpType.add, mybir.AluOpType.subtract
    ctx = ExitStack()
    with ctx:
        def sb(name, cols, dt):
            return ctx.enter_context(nc.sbuf_tensor(name, [P, cols], dt))

        def ps(name):
            return ctx.enter_context(nc.psum_tensor(name, [P, TOKENS], f32))

        def sem(name):
            return ctx.enter_context(nc.semaphore(name))

        x_hi, x_lo = sb("x_hi", CHUNKS * TOKENS, f32r), sb("x_lo", CHUNKS * TOKENS, f32r)
        x_raw = [sb(f"x_raw{i}", GROUP_COLS, f32) for i in range(2)]
        w_raw = [sb(f"w_raw{c}", BLOCK_COLS, f32) for c in range(BLOCKS)]
        w_hi = [sb(f"w_hi{c}", BLOCK_COLS, f32r) for c in range(BLOCKS)]
        w_lo = [sb(f"w_lo{c}", BLOCK_COLS, f32r) for c in range(BLOCKS)]
        y = sb("y", TILES * TOKENS, f32)
        y_hi, y_lo = sb("y_hi", 2 * TOKENS, f32r), sb("y_lo", 2 * TOKENS, f32r)
        b_raw = sb("b_raw", CHUNKS * RANK, f32)
        a_raw = sb("a_raw", FEAT, f32)
        b_parts = [sb(f"b_parts{i}", 2 * P, f32r) for i in range(2)]
        a_parts = [sb(f"a_parts{i}", 2 * P, f32r) for i in range(2)]
        t_parts = sb("t_parts", TOKENS, f32r)
        out_sb = [sb(f"out_sb{i}", 2 * TOKENS, f32) for i in range(2)]

        wx = [[ps(f"wx{i}{t}") for t in range(2)] for i in range(2)]
        bx = ps("bx")
        ta = [ps(f"ta{t}") for t in range(2)]

        x_loaded = [sem(f"x_loaded{i}") for i in range(2)]
        w_loaded = [sem(f"w_loaded{c}") for c in range(BLOCKS)]
        b_loaded, a_loaded = sem("b_loaded"), sem("a_loaded")
        stored = [sem(f"stored{i}") for i in range(2)]
        x_hi_ready, x_lo_ready = sem("x_hi_ready"), sem("x_lo_ready")
        w_hi_ready, w_lo_ready = sem("w_hi_ready"), sem("w_lo_ready")
        blocks_done = sem("blocks_done")
        y_restored, y_ready = sem("y_restored"), sem("y_ready")
        y_hi_ready, y_lo_ready = sem("y_hi_ready"), sem("y_lo_ready")
        b_hi_ready, b_ready = sem("b_hi_ready"), sem("b_ready")
        a_hi_ready, a_ready = sem("a_hi_ready"), sem("a_ready")
        bx_done, ta_done = sem("bx_done"), sem("ta_done")
        t_hi_ready, t_ready = sem("t_hi_ready"), sem("t_ready")
        out_ready = sem("out_ready")
        block = ctx.enter_context(nc.Block())

        def tok(tile):
            return bass.ds(tile * TOKENS, TOKENS)

        def all_rows(eng, row):
            row(0, False, True)
            with eng.Fori(1, BATCH - 1) as b:
                row(b, True, True)
            row(BATCH - 1, True, False)

        @block.sync
        def _(sp):
            def adapter(b):
                return sp.value_load(ids[0:1, bass.ds(b, 1)], min_val=0, max_val=ADAPTERS - 1)

            def load_w(n, c, p, who):
                if not isinstance(n, int) or n >= BLOCKS:
                    sp.wait_ge(w_lo_ready, n - BLOCKS + 1)
                sp.dma_start(w_raw[c][:, :], wT[bass.ds(who, 1), bass.ds(p, 1), c, :, :]
                             .rearrange("a b p n -> p (a b n)")).then_inc(w_loaded[c], 16)

            def load_x(b, g):
                if g >= 2 or not isinstance(b, int) or b > 0:
                    sp.wait_ge(x_lo_ready, b * BLOCKS + g - 1)
                sp.dma_start(x_raw[g % 2][:, :], xT[bass.ds(b, 1), :, g * GROUP_COLS:(g + 1) * GROUP_COLS]
                             .rearrange("b p n -> p (b n)")).then_inc(x_loaded[g % 2], 16)

            def load_b(b, who):
                if not isinstance(b, int) or b > 0:
                    sp.wait_ge(b_ready, b * PAIRS)
                sp.dma_start(b_raw[:, :], bT[bass.ds(who, 1), :, :].rearrange("a p n -> p (a n)")).then_inc(b_loaded, 16)

            def load_a(b, who, prev):
                if prev:
                    sp.wait_ge(a_ready, b * PAIRS)
                for r in range(P // RANK):
                    sp.dma_start(a_raw[r * RANK:(r + 1) * RANK, :],
                                 aT[bass.ds(who, 1), :, :].rearrange("a r n -> r (a n)")).then_inc(a_loaded, 16)

            def store(b, p, u):
                sp.wait_ge(out_ready, (b * PAIRS + p + 1) * 2)
                sp.dma_start(outT[bass.ds(b, 1), :, bass.ds(p * 2 * TOKENS, 2 * TOKENS)]
                             .rearrange("b p n -> p (b n)"), out_sb[u][:, :]).then_inc(stored[u], 16)

            def step(b, p, u, prev, more, this, after):
                S = b * PAIRS + p
                late = isinstance(p, int) and p >= PAIRS - 2
                last = isinstance(p, int) and p == PAIRS - 1
                if not last or more:
                    load_w(S * BLOCKS + 7, 3, 0 if last else p + 1, after if last else this)
                if not late or more:
                    load_w(S * BLOCKS + 8, 0, p - (PAIRS - 2) if late else p + 2, after if late else this)
                    if last:
                        load_x(b + 1, 2)
                    load_w(S * BLOCKS + 9, 1, p - (PAIRS - 2) if late else p + 2, after if late else this)
                    if last:
                        load_x(b + 1, 3)
                if last:
                    load_a(b, this, prev)
                    if more:
                        load_b(b + 1, after)
                if prev:
                    store(b - 1, p, u)
                if not late or more:
                    load_w(S * BLOCKS + 10, 2, p - (PAIRS - 2) if late else p + 2, after if late else this)
                if late and not last and more:
                    load_x(b + 1, 0)
                    load_x(b + 1, 1)

            def row(b, prev, more):
                this = adapter(b)
                with sp.Fori(0, PAIRS // 2 - 1) as q:
                    step(b, q * 2, 0, prev, more, this, None)
                    step(b, q * 2 + 1, 1, prev, more, this, None)
                after = adapter(b + 1) if more else None
                step(b, PAIRS - 2, 0, prev, more, this, after)
                step(b, PAIRS - 1, 1, prev, more, this, after)

            for u in range(2):
                sp.sem_inc(stored[u], 16)
            first = adapter(0)
            load_x(0, 0)
            load_w(0, 0, 0, first)
            load_x(0, 1)
            load_w(1, 1, 0, first)
            load_x(0, 2)
            load_w(2, 2, 0, first)
            load_x(0, 3)
            load_w(3, 3, 0, first)
            load_b(0, first)
            for c in range(BLOCKS - 1):
                load_w(BLOCKS + c, c, 1, first)
            all_rows(sp, row)
            for p in range(PAIRS):
                store(BATCH - 1, p, p % 2)
            for u in range(2):
                sp.wait_ge(stored[u], 16 + 16 * BATCH * PAIRS // 2)

        @block.scalar
        def _(act):
            def copy(out, in_):
                return nc.scalar.activation(out, in_, COPY)

            def split_w(n, c, S):
                if not isinstance(n, int) or n >= BLOCKS:
                    act.wait_ge(blocks_done, n - BLOCKS + 1)
                act.wait_ge(w_loaded[c], S * 16 + 16)
                copy(w_hi[c][:, :], w_raw[c][:, :]).then_inc(w_hi_ready, 1)

            def split_x(b, g):
                if not isinstance(b, int) or b > 0:
                    act.wait_ge(blocks_done, b * (PAIRS * BLOCKS) - BLOCKS + g + 1)
                    act.wait_ge(y_restored, b * TILES - (TILES - KB * (g + 1)))
                act.wait_ge(x_loaded[g % 2], b * 32 + (g // 2 + 1) * 16)
                copy(x_hi[:, g * GROUP_COLS:(g + 1) * GROUP_COLS], x_raw[g % 2][:, :]).then_inc(x_hi_ready, 1)

            def step(b, p, u, prev, more):
                S = b * PAIRS + p
                start = isinstance(S, int) and S == 0
                first = isinstance(p, int) and p == 0
                last = isinstance(p, int) and p == PAIRS - 1
                if not start:
                    if not isinstance(S, int) or S > 1:
                        act.wait_ge(bx_done, S - 1)
                    for t in range(2):
                        act.wait_ge(y_ready, S * 2 - 1 + t)
                        tile = TILES - 2 + t if first else p * 2 - 2 + t
                        copy(y_hi[:, t * TOKENS:(t + 1) * TOKENS], y[:, tok(tile)]).then_inc(y_hi_ready, 1)
                split_w(S * BLOCKS + 3, 3, S)
                if first:
                    split_x(b, 3)
                if not last or more:
                    split_w(S * BLOCKS + 4, 0, S + 1)
                    if last:
                        split_x(b + 1, 0)
                if first:
                    act.wait_ge(b_loaded, b * 16 + 16)
                if not isinstance(S, int) or S > 1:
                    act.wait_ge(bx_done, S - 1)
                copy(b_parts[u][:, :].rearrange("p (k c h r) -> p k c h r", k=2, c=REP, h=2)[:, :, :, 0, :],
                     b_raw[:, bass.ds(p * 2 * RANK, 2 * RANK)].rearrange("p (k c r) -> p k c r", k=2, c=1)
                     .to_broadcast([P, 2, REP, RANK])).then_inc(b_hi_ready, 1)
                if prev:
                    if first:
                        act.wait_ge(a_loaded, b * (16 * P // RANK))
                    copy(a_parts[u][:, :], a_raw[:, bass.ds(p * 2 * P, 2 * P)]).then_inc(a_hi_ready, 1)
                if not last or more:
                    split_w(S * BLOCKS + 5, 1, S + 1)
                    if last:
                        split_x(b + 1, 1)
                if prev and first:
                    split_t(b, S)
                if not last or more:
                    split_w(S * BLOCKS + 6, 2, S + 1)
                    if last:
                        split_x(b + 1, 2)

            def split_t(b, S):
                act.wait_ge(bx_done, S)
                copy(t_parts[:, :], bx[:, :]).then_inc(t_hi_ready, 1)

            def row(b, prev, more):
                for p in range(2):
                    step(b, p, p, prev, more)
                with act.Fori(1, PAIRS // 2 - 1) as q:
                    for u in range(2):
                        step(b, q * 2 + u, u, prev, more)
                for u in range(2):
                    step(b, PAIRS - 2 + u, u, prev, more)

            for g in range(BLOCKS - 1):
                split_x(0, g)
                split_w(g, g, 0)
            all_rows(act, row)
            S = BATCH * PAIRS
            act.wait_ge(bx_done, S - 1)
            for t in range(2):
                act.wait_ge(y_ready, S * 2 - 1 + t)
                copy(y_hi[:, t * TOKENS:(t + 1) * TOKENS], y[:, tok(TILES - 2 + t)]).then_inc(y_hi_ready, 1)
            act.wait_ge(a_loaded, BATCH * (16 * P // RANK))
            split_t(BATCH, S)
            for p in range(PAIRS):
                act.wait_ge(ta_done, S - PAIRS + p - 1)
                copy(a_parts[p % 2][:, :], a_raw[:, p * 2 * P:(p + 1) * 2 * P]).then_inc(a_hi_ready, 1)

        @block.gpsimd
        def _(pool):
            def step(b, p, prev):
                S = b * PAIRS + p
                for t in range(2):
                    if prev:
                        pool.wait_ge(out_ready, (S - PAIRS) * 2 + 1 + t)
                    nc.gpsimd.tensor_tensor(y[:, tok(p * 2 + t)], x_hi[:, tok(p * 2 + t)],
                                            x_lo[:, tok(p * 2 + t)], ADD).then_inc(y_restored, 1)

            def row(b, prev, more):
                if not prev:
                    pool.wait_ge(x_lo_ready, BLOCKS)
                else:
                    pool.wait_ge(x_lo_ready, b * BLOCKS + 1)
                for p in range(2):
                    step(b, p, prev)
                with pool.Fori(2, PAIRS) as p:
                    pool.wait_ge(x_lo_ready, b * BLOCKS + BLOCKS)
                    step(b, p, prev)

            all_rows(pool, row)

        @block.vector
        def _(dve):
            def sub(out, a, b):
                return nc.vector.tensor_tensor(out, a, b, SUB)

            def split_w(n, c):
                dve.wait_ge(w_hi_ready, n + 1)
                sub(w_lo[c][:, :], w_raw[c][:, :], w_hi[c][:, :]).then_inc(w_lo_ready, 1)

            def split_x(b, g):
                dve.wait_ge(x_hi_ready, b * BLOCKS + g + 1)
                cols = slice(g * GROUP_COLS, (g + 1) * GROUP_COLS)
                sub(x_lo[:, cols], x_raw[g % 2][:, :], x_hi[:, cols]).then_inc(x_lo_ready, 1)

            def finish_y(S, tiles, u):
                dve.wait_ge(blocks_done, S * BLOCKS)
                for t in range(2):
                    dve.wait_ge(y_restored, S * 2 - 1 + t)
                    here = y[:, tok(tiles + t)]
                    nc.vector.tensor_tensor(here, wx[1 - u][t][:, :], here, ADD).then_inc(y_ready, 1)

            def split_y(S, tiles):
                for t in range(2):
                    dve.wait_ge(y_hi_ready, S * 2 - 1 + t)
                    cols = slice(t * TOKENS, (t + 1) * TOKENS)
                    sub(y_lo[:, cols], y[:, tok(tiles + t)], y_hi[:, cols]).then_inc(y_lo_ready, 1)

            def split_t(b):
                dve.wait_ge(t_hi_ready, b)
                for q in (1, 3):
                    rows = slice(32 * q, 32 * q + 32)
                    last = sub(t_parts[rows, :], bx[rows, :], t_parts[rows, :])
                last.then_inc(t_ready, 1)

            def split_a(S, u):
                p = S[1]
                dve.wait_ge(a_hi_ready, S[0] + 1)
                sub(a_parts[u][HALF:P, :], a_raw[HALF:P, bass.ds(p * 2 * P, 2 * P)],
                    a_parts[u][HALF:P, :]).then_inc(a_ready, 1)

            def add_out(n, p, u):
                dve.wait_ge(ta_done, n + 1)
                dve.wait_ge(stored[u], free_after(n, u))
                for t in range(2):
                    nc.vector.tensor_tensor(out_sb[u][:, t * TOKENS:(t + 1) * TOKENS], ta[t][:, :],
                                            y[:, tok(p * 2 + t)], ADD).then_inc(out_ready, 1)

            def free_after(n, u):
                return (n - u) * 8 + 16

            def step(b, p, u, prev, more):
                S = b * PAIRS + p
                start = isinstance(S, int) and S == 0
                first = isinstance(p, int) and p == 0
                last = isinstance(p, int) and p == PAIRS - 1
                before = TILES - 2 if first else p * 2 - 2
                if not start:
                    finish_y(S, before, u)
                    split_y(S, before)
                split_w(S * BLOCKS + 3, 3)
                if first:
                    split_x(b, 3)
                if not last or more:
                    split_w(S * BLOCKS + 4, 0)
                    if last:
                        split_x(b + 1, 0)
                dve.wait_ge(b_hi_ready, S + 1)
                parts = b_parts[u][:, :].rearrange("p (k c h r) -> p k c h r", k=2, c=REP, h=2)
                sub(parts[:, :, :, 1, :],
                    b_raw[:, bass.ds(p * 2 * RANK, 2 * RANK)].rearrange("p (k c r) -> p k c r", k=2, c=1)
                    .to_broadcast([P, 2, REP, RANK]), parts[:, :, :, 0, :]).then_inc(b_ready, 1)
                if prev:
                    split_a((S - PAIRS, p), u)
                if prev and first:
                    split_t(b)
                if not last or more:
                    split_w(S * BLOCKS + 5, 1)
                    if last:
                        split_x(b + 1, 1)
                if prev:
                    add_out(S - PAIRS, p, u)
                if not last or more:
                    split_w(S * BLOCKS + 6, 2)
                    if last:
                        split_x(b + 1, 2)

            def row(b, prev, more):
                for p in range(2):
                    step(b, p, p, prev, more)
                with dve.Fori(1, PAIRS // 2 - 1) as q:
                    for u in range(2):
                        step(b, q * 2 + u, u, prev, more)
                for u in range(2):
                    step(b, PAIRS - 2 + u, u, prev, more)

            for g in range(BLOCKS - 1):
                split_x(0, g)
                split_w(g, g)
            all_rows(dve, row)
            S = BATCH * PAIRS
            finish_y(S, TILES - 2, 0)
            split_y(S, TILES - 2)
            split_t(BATCH)
            for p in range(PAIRS):
                split_a((S - PAIRS + p, p), p % 2)
                add_out(S - PAIRS + p, p, p % 2)

        @block.tensor
        def _(pe):
            def times_b(S, u, is_first, is_last):
                pe.wait_ge(b_ready, S)
                pe.wait_ge(y_lo_ready, S * 2)
                for t in range(2):
                    for n, part in enumerate((y_hi, y_lo)):
                        last = nc.tensor.matmul(bx[:, :], b_parts[1 - u][:, t * P:(t + 1) * P],
                                                part[:, t * TOKENS:(t + 1) * TOKENS],
                                                start=is_first and t == 0 and n == 0,
                                                stop=is_last and t == 1 and n == 1)
                last.then_inc(bx_done, 1)

            def times_a(n, u, first):
                pe.wait_ge(a_ready, n + 1)
                if not first:
                    pe.wait_ge(out_ready, n * 2)
                for t in range(2):
                    last = nc.tensor.matmul(ta[t][:, :], a_parts[u][:, t * P:(t + 1) * P], t_parts[:, :],
                                            start=True, stop=True)
                last.then_inc(ta_done, 1)

            def step(b, p, u, prev):
                S = b * PAIRS + p
                start = isinstance(S, int) and S == 0
                first = isinstance(p, int) and p == 0
                second = isinstance(p, int) and p == 1
                if not isinstance(S, int) or S >= 2:
                    pe.wait_ge(y_ready, S * 2 - 2)
                for c in range(BLOCKS):
                    if first:
                        pe.wait_ge(x_lo_ready, b * BLOCKS + c + 1)
                    pe.wait_ge(w_lo_ready, S * BLOCKS + c + 1)
                    for kk in range(KB):
                        k = c * KB + kk
                        if k == BX_AT and not start:
                            if second and prev:
                                pe.wait_ge(t_ready, b)
                            times_b(S, u, second, first)
                        if k == A_AT and prev:
                            if first:
                                pe.wait_ge(t_ready, b)
                            times_a(S - PAIRS, u, first)
                        cols = slice(k * TOKENS, (k + 1) * TOKENS)
                        for t in range(2):
                            own = slice((kk * 2 + t) * P, (kk * 2 + t + 1) * P)
                            for n, (w, x) in enumerate(((w_hi, x_hi), (w_hi, x_lo), (w_lo, x_hi))):
                                last = nc.tensor.matmul(wx[u][t][:, :], w[c][:, own], x[:, cols],
                                                        start=k == 0 and n == 0, stop=k == CHUNKS - 1 and n == 2)
                    last.then_inc(blocks_done, 1)

            def row(b, prev):
                for p in range(2):
                    step(b, p, p, prev)
                with pe.Fori(1, PAIRS // 2) as q:
                    for u in range(2):
                        step(b, q * 2 + u, u, prev)

            row(0, False)
            with pe.Fori(1, BATCH) as b:
                row(b, True)
            S = BATCH * PAIRS
            times_b(S, 0, False, True)
            pe.wait_ge(t_ready, BATCH)
            for p in range(PAIRS):
                times_a(S - PAIRS + p, p % 2, p == 0)


def kernel(x, itok_B_3_7, L0_cond_weight, L1_cond_A, L1_cond_B):
    import concourse.bacc as bacc
    from concourse.bass_utils import run_bass_kernel_spmd

    def lay(a, split, order, shape):
        return np.ascontiguousarray(np.asarray(a).reshape(split).transpose(order)).reshape(shape)

    arrays = {
        "ids": np.ascontiguousarray(np.asarray(itok_B_3_7)).reshape(1, BATCH),
        "xT": lay(x, (BATCH, TOKENS, CHUNKS, P), (0, 3, 2, 1), (BATCH, P, CHUNKS * TOKENS)),
        "wT": lay(L0_cond_weight, (ADAPTERS, PAIRS, 2 * P, BLOCKS, KB, P), (0, 1, 3, 5, 4, 2),
                  (ADAPTERS, PAIRS, BLOCKS, P, BLOCK_COLS)),
        "bT": lay(L1_cond_B, (ADAPTERS, RANK, CHUNKS, P), (0, 3, 2, 1), (ADAPTERS, P, CHUNKS * RANK)),
        "aT": lay(L1_cond_A, (ADAPTERS, FEAT, RANK), (0, 2, 1), (ADAPTERS, RANK, FEAT)),
    }
    nc = bacc.Bacc("TRN2", target_bir_lowering=False, num_devices=1)
    args = [nc.dram_tensor(n, a.shape, mybir.dt.from_np(a.dtype), kind="ExternalInput").ap() for n, a in arrays.items()]
    out = nc.dram_tensor("outT", (BATCH, P, TILES * TOKENS), mybir.dt.float32, kind="ExternalOutput").ap()
    low_rank_chain(nc, *args, out)
    r = run_bass_kernel_spmd(nc, [arrays], core_ids=[0])
    got = r.results[0]["outT"].reshape(BATCH, P, TILES, TOKENS).transpose(0, 3, 2, 1)
    return np.ascontiguousarray(got).reshape(BATCH, TOKENS, FEAT)
```

```python
import numpy as np
import concourse.bass as bass
from concourse import mybir
from contextlib import ExitStack

P = 128
BATCH, TOKENS, FEAT = 8, 512, 2048
ADAPTERS, RANK = 8, 16
TILES = FEAT // P
CHUNKS = FEAT // P
PAIRS = TILES // 2
BLOCKS = 4
KB = CHUNKS // BLOCKS
BLOCK_COLS = KB * 2 * P
GROUP_COLS = KB * TOKENS
REP = P // (2 * RANK)
HALF = P // 2
PIECES = KB - 1
TAIL_TURN = 3
BX_AT, A_AT = 6, 11


def low_rank_chain(nc, ids, xT, wT, bT, aT, outT):
    f32, f32r = mybir.dt.float32, mybir.dt.float32r
    COPY = mybir.ActivationFunctionType.Copy
    ADD, SUB = mybir.AluOpType.add, mybir.AluOpType.subtract
    ctx = ExitStack()
    with ctx:
        def sb(name, cols, dt):
            return ctx.enter_context(nc.sbuf_tensor(name, [P, cols], dt))

        def ps(name):
            return ctx.enter_context(nc.psum_tensor(name, [P, TOKENS], f32))

        def sem(name):
            return ctx.enter_context(nc.semaphore(name))

        x_hi, x_lo = sb("x_hi", CHUNKS * TOKENS, f32r), sb("x_lo", CHUNKS * TOKENS, f32r)
        x_raw = [sb(f"x_raw{i}", GROUP_COLS, f32) for i in range(2)]
        w_raw = [sb(f"w_raw{c}", BLOCK_COLS, f32) for c in range(BLOCKS)]
        w_hi = [sb(f"w_hi{c}", BLOCK_COLS, f32r) for c in range(BLOCKS)]
        w_lo = [sb(f"w_lo{c}", BLOCK_COLS, f32r) for c in range(BLOCKS)]
        y = sb("y", TILES * TOKENS, f32)
        y_hi, y_lo = sb("y_hi", 2 * TOKENS, f32r), sb("y_lo", 2 * TOKENS, f32r)
        b_raw = sb("b_raw", CHUNKS * RANK, f32)
        a_raw = sb("a_raw", FEAT, f32)
        b_parts = [sb(f"b_parts{i}", 2 * P, f32r) for i in range(2)]
        a_parts = [sb(f"a_parts{i}", 2 * P, f32r) for i in range(2)]
        t_parts = sb("t_parts", TOKENS, f32r)
        out_sb = [sb(f"out_sb{i}", 2 * TOKENS, f32) for i in range(2)]

        wx = [[ps(f"wx{i}{t}") for t in range(2)] for i in range(2)]
        bx = ps("bx")
        ta = [ps(f"ta{t}") for t in range(2)]

        x_loaded = [sem(f"x_loaded{i}") for i in range(2)]
        w_loaded = [sem(f"w_loaded{c}") for c in range(BLOCKS)]
        b_loaded, a_loaded = sem("b_loaded"), sem("a_loaded")
        stored = [sem(f"stored{i}") for i in range(2)]
        x_hi_ready, x_lo_ready = sem("x_hi_ready"), sem("x_lo_ready")
        w_hi_ready, w_lo_ready = sem("w_hi_ready"), sem("w_lo_ready")
        blocks_done = sem("blocks_done")
        y_restored, y_ready = sem("y_restored"), sem("y_ready")
        y_hi_ready, y_lo_ready = sem("y_hi_ready"), sem("y_lo_ready")
        b_hi_ready, b_ready = sem("b_hi_ready"), sem("b_ready")
        a_hi_ready, a_ready = sem("a_hi_ready"), sem("a_ready")
        bx_done, ta_done = sem("bx_done"), sem("ta_done")
        t_hi_ready, t_ready = sem("t_hi_ready"), sem("t_ready")
        out_ready = sem("out_ready")
        piece_loaded = [sem(f"piece_loaded{k}") for k in range(CHUNKS)]
        piece_x_hi, piece_x_lo = sem("piece_x_hi"), sem("piece_x_lo")
        piece_w_hi, piece_w_lo = sem("piece_w_hi"), sem("piece_w_lo")
        tail_ta_done = sem("tail_ta_done")
        tail_vector_ready, tail_scalar_read, tail_pool_ready = sem("tail_vector_ready"), sem("tail_scalar_read"), sem("tail_pool_ready")
        tail_stored = sem("tail_stored")
        block = ctx.enter_context(nc.Block())

        def tok(tile):
            return bass.ds(tile * TOKENS, TOKENS)

        def piece(k):
            c, kk = divmod(k, KB)
            return c, kk, slice(k * TOKENS, (k + 1) * TOKENS), slice(kk * 2 * P, (kk + 1) * 2 * P)

        def tail_a(tile):
            return w_hi[tile // 8][:, (tile % 8) * P:(tile % 8 + 1) * P]

        tail_banks = [ta[0], ta[1], wx[0][0], wx[0][1], wx[1][0], wx[1][1]]

        def tail_sb(n):
            return x_raw[n // KB][:, (n % KB) * TOKENS:(n % KB + 1) * TOKENS]

        def scalar_turns(tile):
            return tile // TAIL_TURN

        def all_rows(eng, row):
            row(0, False, True)
            with eng.Fori(1, BATCH - 1) as b:
                row(b, True, True)
            row(BATCH - 1, True, False)

        @block.sync
        def _(sp):
            def adapter(b):
                return sp.value_load(ids[0:1, bass.ds(b, 1)], min_val=0, max_val=ADAPTERS - 1)

            def load_w(n, c, p, who):
                sp.wait_ge(w_lo_ready, n - BLOCKS + 1)
                sp.dma_start(w_raw[c][:, :], wT[bass.ds(who, 1), bass.ds(p, 1), c, :, :]
                             .rearrange("a b p n -> p (a b n)")).then_inc(w_loaded[c], 16)

            def load_x(b, g):
                sp.wait_ge(x_lo_ready, b * BLOCKS + g - 1)
                sp.dma_start(x_raw[g % 2][:, :], xT[bass.ds(b, 1), :, g * GROUP_COLS:(g + 1) * GROUP_COLS]
                             .rearrange("b p n -> p (b n)")).then_inc(x_loaded[g % 2], 16)

            def load_b(b, who):
                if not isinstance(b, int) or b > 0:
                    sp.wait_ge(b_ready, b * PAIRS)
                sp.dma_start(b_raw[:, :], bT[bass.ds(who, 1), :, :].rearrange("a p n -> p (a n)")).then_inc(b_loaded, 16)

            def load_a(b, who, prev):
                if prev:
                    sp.wait_ge(a_ready, b * PAIRS)
                for r in range(P // RANK):
                    sp.dma_start(a_raw[r * RANK:(r + 1) * RANK, :],
                                 aT[bass.ds(who, 1), :, :].rearrange("a r n -> r (a n)")).then_inc(a_loaded, 16)

            def store(b, p, u):
                sp.wait_ge(out_ready, (b * PAIRS + p + 1) * 2)
                sp.dma_start(outT[bass.ds(b, 1), :, bass.ds(p * 2 * TOKENS, 2 * TOKENS)]
                             .rearrange("b p n -> p (b n)"), out_sb[u][:, :]).then_inc(stored[u], 16)

            def step(b, p, u, prev, more, this, after):
                S = b * PAIRS + p
                late = isinstance(p, int) and p >= PAIRS - 2
                last = isinstance(p, int) and p == PAIRS - 1
                if not last or more:
                    load_w(S * BLOCKS + 7, 3, 0 if last else p + 1, after if last else this)
                if not late or more:
                    load_w(S * BLOCKS + 8, 0, p - (PAIRS - 2) if late else p + 2, after if late else this)
                    if last:
                        load_x(b + 1, 2)
                    load_w(S * BLOCKS + 9, 1, p - (PAIRS - 2) if late else p + 2, after if late else this)
                    if last:
                        load_x(b + 1, 3)
                if last:
                    load_a(b, this, prev)
                    if more:
                        load_b(b + 1, after)
                if prev:
                    store(b - 1, p, u)
                if not late or more:
                    load_w(S * BLOCKS + 10, 2, p - (PAIRS - 2) if late else p + 2, after if late else this)
                if late and not last and more:
                    load_x(b + 1, 0)
                    load_x(b + 1, 1)

            def row(b, prev, more):
                this = adapter(b)
                with sp.Fori(0, PAIRS // 2 - 1) as q:
                    step(b, q * 2, 0, prev, more, this, None)
                    step(b, q * 2 + 1, 1, prev, more, this, None)
                after = adapter(b + 1) if more else None
                step(b, PAIRS - 2, 0, prev, more, this, after)
                step(b, PAIRS - 1, 1, prev, more, this, after)

            for u in range(2):
                sp.sem_inc(stored[u], 16)
            for k in range(CHUNKS):
                c, kk, cols, own = piece(k)
                sp.dma_start(y[:, cols], xT[0, :, cols]).then_inc(piece_loaded[k], 16)
                if k == 0:
                    first = adapter(0)
                sp.dma_start(w_raw[c][:, own], wT[bass.ds(first, 1), 0, c, :, own]
                             .rearrange("a p n -> p (a n)")).then_inc(piece_loaded[k], 16)
            load_b(0, first)
            for c in range(BLOCKS - 1):
                load_w(BLOCKS + c, c, 1, first)
            all_rows(sp, row)
            for p in range(PAIRS):
                by_scalar = scalar_turns(p * 2 + 2)
                sp.wait_ge(tail_vector_ready, p * 2 + 2 - by_scalar)
                if by_scalar:
                    sp.wait_ge(tail_pool_ready, by_scalar)
                cols = slice(p * 2 * TOKENS, (p + 1) * 2 * TOKENS)
                sp.dma_start(outT[BATCH - 1, :, cols], y[:, cols]).then_inc(tail_stored, 16)
            for u in range(2):
                sp.wait_ge(stored[u], 16 + 16 * (BATCH - 1) * PAIRS // 2)
            sp.wait_ge(tail_stored, 16 * PAIRS)

        @block.scalar
        def _(act):
            def copy(out, in_):
                return nc.scalar.activation(out, in_, COPY)

            def split_w(n, c, S):
                act.wait_ge(blocks_done, n - BLOCKS + 1)
                act.wait_ge(w_loaded[c], S * 16)
                copy(w_hi[c][:, :], w_raw[c][:, :]).then_inc(w_hi_ready, 1)

            def split_x(b, g):
                act.wait_ge(blocks_done, b * (PAIRS * BLOCKS) - BLOCKS + g + 1)
                act.wait_ge(y_restored, b * TILES - (TILES - KB * (g + 1)))
                act.wait_ge(x_loaded[g % 2], b * 32 - 32 + (g // 2 + 1) * 16)
                copy(x_hi[:, g * GROUP_COLS:(g + 1) * GROUP_COLS], x_raw[g % 2][:, :]).then_inc(x_hi_ready, 1)

            def step(b, p, u, prev, more):
                S = b * PAIRS + p
                start = isinstance(S, int) and S == 0
                first = isinstance(p, int) and p == 0
                last = isinstance(p, int) and p == PAIRS - 1
                if not start:
                    if not isinstance(S, int) or S > 1:
                        act.wait_ge(bx_done, S - 1)
                    for t in range(2):
                        act.wait_ge(y_ready, S * 2 - 1 + t)
                        tile = TILES - 2 + t if first else p * 2 - 2 + t
                        copy(y_hi[:, t * TOKENS:(t + 1) * TOKENS], y[:, tok(tile)]).then_inc(y_hi_ready, 1)
                if not start:
                    split_w(S * BLOCKS + 3, 3, S)
                if first and not start:
                    split_x(b, 3)
                if not last or more:
                    split_w(S * BLOCKS + 4, 0, S + 1)
                    if last:
                        split_x(b + 1, 0)
                if first:
                    act.wait_ge(b_loaded, b * 16 + 16)
                if not isinstance(S, int) or S > 1:
                    act.wait_ge(bx_done, S - 1)
                copy(b_parts[u][:, :].rearrange("p (k c h r) -> p k c h r", k=2, c=REP, h=2)[:, :, :, 0, :],
                     b_raw[:, bass.ds(p * 2 * RANK, 2 * RANK)].rearrange("p (k c r) -> p k c r", k=2, c=1)
                     .to_broadcast([P, 2, REP, RANK])).then_inc(b_hi_ready, 1)
                if prev:
                    if first:
                        act.wait_ge(a_loaded, b * (16 * P // RANK))
                    copy(a_parts[u][:, :], a_raw[:, bass.ds(p * 2 * P, 2 * P)]).then_inc(a_hi_ready, 1)
                if not last or more:
                    split_w(S * BLOCKS + 5, 1, S + 1)
                    if last:
                        split_x(b + 1, 1)
                if prev and first:
                    split_t(b, S)
                if not last or more:
                    split_w(S * BLOCKS + 6, 2, S + 1)
                    if last:
                        split_x(b + 1, 2)

            def split_t(b, S):
                act.wait_ge(bx_done, S)
                copy(t_parts[:, :], bx[:, :]).then_inc(t_hi_ready, 1)

            def row(b, prev, more):
                for p in range(2):
                    step(b, p, p, prev, more)
                with act.Fori(1, PAIRS // 2 - 1) as q:
                    for u in range(2):
                        step(b, q * 2 + u, u, prev, more)
                for u in range(2):
                    step(b, PAIRS - 2 + u, u, prev, more)

            for k in range(CHUNKS):
                c, kk, cols, own = piece(k)
                act.wait_ge(piece_loaded[k], 32)
                copy(x_hi[:, cols], y[:, cols]).then_inc(piece_x_hi if kk < PIECES else x_hi_ready, 1)
                copy(w_hi[c][:, own], w_raw[c][:, own]).then_inc(piece_w_hi if kk < PIECES else w_hi_ready, 1)
            all_rows(act, row)
            S = BATCH * PAIRS
            act.wait_ge(a_loaded, BATCH * (16 * P // RANK))
            for h in range(2):
                act.wait_ge(blocks_done, S * BLOCKS - BLOCKS + h + 1)
                copy(w_hi[h][:, :], a_raw[:, h * BLOCK_COLS:(h + 1) * BLOCK_COLS]).then_inc(a_hi_ready, 1)
            act.wait_ge(bx_done, S - 1)
            for t in range(2):
                act.wait_ge(y_ready, S * 2 - 1 + t)
                copy(y_hi[:, t * TOKENS:(t + 1) * TOKENS], y[:, tok(TILES - 2 + t)]).then_inc(y_hi_ready, 1)
            split_t(BATCH, S)
            for n, tile in enumerate(range(TAIL_TURN - 1, TILES, TAIL_TURN)):
                act.wait_ge(tail_ta_done, tile + 1)
                copy(tail_sb(n), tail_banks[tile % len(tail_banks)][:, :]).then_inc(tail_scalar_read, 1)

        @block.gpsimd
        def _(pool):
            def step(b, p):
                for t in range(2):
                    pool.wait_ge(out_ready, (b * PAIRS + p - PAIRS) * 2 + 1 + t)
                    nc.gpsimd.tensor_tensor(y[:, tok(p * 2 + t)], x_hi[:, tok(p * 2 + t)],
                                            x_lo[:, tok(p * 2 + t)], ADD).then_inc(y_restored, 1)

            def row(b):
                pool.wait_ge(x_lo_ready, b * BLOCKS + 1)
                for p in range(2):
                    step(b, p)
                with pool.Fori(2, PAIRS) as p:
                    pool.wait_ge(x_lo_ready, b * BLOCKS + BLOCKS)
                    step(b, p)

            for k in range(CHUNKS):
                pool.wait_ge(piece_loaded[k], 32)
            pool.sem_inc(y_restored, TILES)
            with pool.Fori(1, BATCH) as b:
                row(b)
            for n, tile in enumerate(range(TAIL_TURN - 1, TILES, TAIL_TURN)):
                pool.wait_ge(tail_scalar_read, n + 1)
                here = y[:, tok(tile)]
                nc.gpsimd.tensor_tensor(here, tail_sb(n), here, ADD).then_inc(tail_pool_ready, 1)

        @block.vector
        def _(dve):
            def sub(out, a, b):
                return nc.vector.tensor_tensor(out, a, b, SUB)

            def split_w(n, c):
                dve.wait_ge(w_hi_ready, n + 1)
                sub(w_lo[c][:, :], w_raw[c][:, :], w_hi[c][:, :]).then_inc(w_lo_ready, 1)

            def split_x(b, g):
                dve.wait_ge(x_hi_ready, b * BLOCKS + g + 1)
                cols = slice(g * GROUP_COLS, (g + 1) * GROUP_COLS)
                sub(x_lo[:, cols], x_raw[g % 2][:, :], x_hi[:, cols]).then_inc(x_lo_ready, 1)

            def finish_y(S, tiles, u):
                dve.wait_ge(blocks_done, S * BLOCKS)
                for t in range(2):
                    dve.wait_ge(y_restored, S * 2 - 1 + t)
                    here = y[:, tok(tiles + t)]
                    nc.vector.tensor_tensor(here, wx[1 - u][t][:, :], here, ADD).then_inc(y_ready, 1)

            def split_y(S, tiles):
                for t in range(2):
                    dve.wait_ge(y_hi_ready, S * 2 - 1 + t)
                    cols = slice(t * TOKENS, (t + 1) * TOKENS)
                    sub(y_lo[:, cols], y[:, tok(tiles + t)], y_hi[:, cols]).then_inc(y_lo_ready, 1)

            def split_t(b):
                dve.wait_ge(t_hi_ready, b)
                for q in (1, 3):
                    rows = slice(32 * q, 32 * q + 32)
                    last = sub(t_parts[rows, :], bx[rows, :], t_parts[rows, :])
                last.then_inc(t_ready, 1)

            def split_a(n, p, u):
                dve.wait_ge(a_hi_ready, n + 1)
                sub(a_parts[u][HALF:P, :], a_raw[HALF:P, bass.ds(p * 2 * P, 2 * P)],
                    a_parts[u][HALF:P, :]).then_inc(a_ready, 1)

            def add_out(n, p, u):
                dve.wait_ge(ta_done, n + 1)
                dve.wait_ge(stored[u], free_after(n, u))
                for t in range(2):
                    nc.vector.tensor_tensor(out_sb[u][:, t * TOKENS:(t + 1) * TOKENS], ta[t][:, :],
                                            y[:, tok(p * 2 + t)], ADD).then_inc(out_ready, 1)

            def free_after(n, u):
                return (n - u) * 8 + 16

            def step(b, p, u, prev, more):
                S = b * PAIRS + p
                start = isinstance(S, int) and S == 0
                first = isinstance(p, int) and p == 0
                last = isinstance(p, int) and p == PAIRS - 1
                before = TILES - 2 if first else p * 2 - 2
                if not start:
                    finish_y(S, before, u)
                    split_y(S, before)
                if not start:
                    split_w(S * BLOCKS + 3, 3)
                if first and not start:
                    split_x(b, 3)
                if not last or more:
                    split_w(S * BLOCKS + 4, 0)
                    if last:
                        split_x(b + 1, 0)
                dve.wait_ge(b_hi_ready, S + 1)
                parts = b_parts[u][:, :].rearrange("p (k c h r) -> p k c h r", k=2, c=REP, h=2)
                sub(parts[:, :, :, 1, :],
                    b_raw[:, bass.ds(p * 2 * RANK, 2 * RANK)].rearrange("p (k c r) -> p k c r", k=2, c=1)
                    .to_broadcast([P, 2, REP, RANK]), parts[:, :, :, 0, :]).then_inc(b_ready, 1)
                if prev:
                    split_a(S - PAIRS, p, u)
                if prev and first:
                    split_t(b)
                if not last or more:
                    split_w(S * BLOCKS + 5, 1)
                    if last:
                        split_x(b + 1, 1)
                if prev:
                    add_out(S - PAIRS, p, u)
                if not last or more:
                    split_w(S * BLOCKS + 6, 2)
                    if last:
                        split_x(b + 1, 2)

            def row(b, prev, more):
                for p in range(2):
                    step(b, p, p, prev, more)
                with dve.Fori(1, PAIRS // 2 - 1) as q:
                    for u in range(2):
                        step(b, q * 2 + u, u, prev, more)
                for u in range(2):
                    step(b, PAIRS - 2 + u, u, prev, more)

            for k in range(CHUNKS):
                c, kk, cols, own = piece(k)
                dve.wait_ge(*((piece_x_hi, c * PIECES + kk + 1) if kk < PIECES else (x_hi_ready, c + 1)))
                sub(x_lo[:, cols], y[:, cols], x_hi[:, cols]).then_inc(piece_x_lo if kk < PIECES else x_lo_ready, 1)
                dve.wait_ge(*((piece_w_hi, c * PIECES + kk + 1) if kk < PIECES else (w_hi_ready, c + 1)))
                sub(w_lo[c][:, own], w_raw[c][:, own], w_hi[c][:, own]).then_inc(
                    piece_w_lo if kk < PIECES else w_lo_ready, 1)
            all_rows(dve, row)
            S = BATCH * PAIRS
            for h in range(2):
                dve.wait_ge(a_hi_ready, S - PAIRS + h + 1)
                low = w_hi[h][HALF:P, :]
                sub(low, a_raw[HALF:P, h * BLOCK_COLS:(h + 1) * BLOCK_COLS], low).then_inc(a_ready, 1)
            finish_y(S, TILES - 2, 0)
            split_y(S, TILES - 2)
            split_t(BATCH)
            for tile in range(TILES):
                if tile % TAIL_TURN != TAIL_TURN - 1:
                    dve.wait_ge(tail_ta_done, tile + 1)
                    here = y[:, tok(tile)]
                    nc.vector.tensor_tensor(here, tail_banks[tile % len(tail_banks)][:, :], here, ADD).then_inc(tail_vector_ready, 1)

        @block.tensor
        def _(pe):
            def times_b(S, u, is_first, is_last):
                pe.wait_ge(b_ready, S)
                pe.wait_ge(y_lo_ready, S * 2)
                for t in range(2):
                    for n, part in enumerate((y_hi, y_lo)):
                        last = nc.tensor.matmul(bx[:, :], b_parts[1 - u][:, t * P:(t + 1) * P],
                                                part[:, t * TOKENS:(t + 1) * TOKENS],
                                                start=is_first and t == 0 and n == 0,
                                                stop=is_last and t == 1 and n == 1)
                last.then_inc(bx_done, 1)

            def times_a(n, u, first):
                pe.wait_ge(a_ready, n + 1)
                if not first:
                    pe.wait_ge(out_ready, n * 2)
                for t in range(2):
                    last = nc.tensor.matmul(ta[t][:, :], a_parts[u][:, t * P:(t + 1) * P], t_parts[:, :],
                                            start=True, stop=True)
                last.then_inc(ta_done, 1)

            def step(b, p, u, prev):
                S = b * PAIRS + p
                start = isinstance(S, int) and S == 0
                first = isinstance(p, int) and p == 0
                second = isinstance(p, int) and p == 1
                if not isinstance(S, int) or S >= 2:
                    pe.wait_ge(y_ready, S * 2 - 2)
                for c in range(BLOCKS):
                    if first and not start:
                        pe.wait_ge(x_lo_ready, b * BLOCKS + c + 1)
                    if not start:
                        pe.wait_ge(w_lo_ready, S * BLOCKS + c + 1)
                    for kk in range(KB):
                        k = c * KB + kk
                        if start:
                            pe.wait_ge(*((piece_x_lo, c * PIECES + kk + 1) if kk < PIECES else (x_lo_ready, c + 1)))
                            pe.wait_ge(*((piece_w_lo, c * PIECES + kk + 1) if kk < PIECES else (w_lo_ready, c + 1)))
                        if k == BX_AT and not start:
                            if second and prev:
                                pe.wait_ge(t_ready, b)
                            times_b(S, u, second, first)
                        if k == A_AT and prev:
                            if first:
                                pe.wait_ge(t_ready, b)
                            times_a(S - PAIRS, u, first)
                        cols = slice(k * TOKENS, (k + 1) * TOKENS)
                        for t in range(2):
                            own = slice((kk * 2 + t) * P, (kk * 2 + t + 1) * P)
                            for n, (w, x) in enumerate(((w_hi, x_hi), (w_hi, x_lo), (w_lo, x_hi))):
                                last = nc.tensor.matmul(wx[u][t][:, :], w[c][:, own], x[:, cols],
                                                        start=k == 0 and n == 0, stop=k == CHUNKS - 1 and n == 2)
                    last.then_inc(blocks_done, 1)

            def row(b, prev):
                for p in range(2):
                    step(b, p, p, prev)
                with pe.Fori(1, PAIRS // 2) as q:
                    for u in range(2):
                        step(b, q * 2 + u, u, prev)

            row(0, False)
            with pe.Fori(1, BATCH) as b:
                row(b, True)
            S = BATCH * PAIRS
            times_b(S, 0, False, True)
            pe.wait_ge(a_ready, S - PAIRS + 2)
            pe.wait_ge(out_ready, (S - PAIRS) * 2)
            pe.wait_ge(t_ready, BATCH)
            for tile in range(TILES):
                before = tile - len(tail_banks)
                if before >= 0 and before % TAIL_TURN == TAIL_TURN - 1:
                    pe.wait_ge(tail_scalar_read, scalar_turns(before) + 1)
                elif before >= 0:
                    pe.wait_ge(tail_vector_ready, before + 1 - scalar_turns(before))
                nc.tensor.matmul(tail_banks[tile % len(tail_banks)][:, :], tail_a(tile), t_parts[:, :],
                                 start=True, stop=True).then_inc(tail_ta_done, 1)


def kernel(x, itok_B_3_7, L0_cond_weight, L1_cond_A, L1_cond_B):
    import concourse.bacc as bacc
    from concourse.bass_utils import run_bass_kernel_spmd

    def lay(a, split, order, shape):
        return np.ascontiguousarray(np.asarray(a).reshape(split).transpose(order)).reshape(shape)

    arrays = {
        "ids": np.ascontiguousarray(np.asarray(itok_B_3_7)).reshape(1, BATCH),
        "xT": lay(x, (BATCH, TOKENS, CHUNKS, P), (0, 3, 2, 1), (BATCH, P, CHUNKS * TOKENS)),
        "wT": lay(L0_cond_weight, (ADAPTERS, PAIRS, 2 * P, BLOCKS, KB, P), (0, 1, 3, 5, 4, 2),
                  (ADAPTERS, PAIRS, BLOCKS, P, BLOCK_COLS)),
        "bT": lay(L1_cond_B, (ADAPTERS, RANK, CHUNKS, P), (0, 3, 2, 1), (ADAPTERS, P, CHUNKS * RANK)),
        "aT": lay(L1_cond_A, (ADAPTERS, FEAT, RANK), (0, 2, 1), (ADAPTERS, RANK, FEAT)),
    }
    nc = bacc.Bacc("TRN2", target_bir_lowering=False, num_devices=1)
    args = [nc.dram_tensor(n, a.shape, mybir.dt.from_np(a.dtype), kind="ExternalInput").ap() for n, a in arrays.items()]
    out = nc.dram_tensor("outT", (BATCH, P, TILES * TOKENS), mybir.dt.float32, kind="ExternalOutput").ap()
    low_rank_chain(nc, *args, out)
    r = run_bass_kernel_spmd(nc, [arrays], core_ids=[0])
    got = r.results[0]["outT"].reshape(BATCH, P, TILES, TOKENS).transpose(0, 3, 2, 1)
    return np.ascontiguousarray(got).reshape(BATCH, TOKENS, FEAT)
```
